# Optimizing a Trainium2 kernel written in Bass

```python
import numpy as np
import jax
import jax.numpy as jnp

def _softmax(x, axis=-1):
    return jax.nn.softmax(x, axis=axis)

def _gelu(x):
    return jax.nn.gelu(x, approximate=True)

def _silu(x):
    return jax.nn.silu(x)

def _sigmoid(x):
    return jax.nn.sigmoid(x)

def _layernorm(x, axis=-1, eps=1e-05):
    m = jnp.mean(x, axis=axis, keepdims=True)
    v = jnp.var(x, axis=axis, keepdims=True)
    return (x - m) / jnp.sqrt(v + eps)

def _scatter_add(tgt, idx, src, axis=0):
    return tgt.at[idx].add(src)

def _segment_sum(src, seg, n):
    return jax.ops.segment_sum(src, seg, n)
kernel_name = 'mk_adj_preln_d1_adj_r2_ec07cc'

def setup_inputs(seed: int=0):
    np.random.seed(seed)
    _w = jnp.asarray

    def _rec_inputs():
        import jax
        import jax.numpy as jnp
        _gk = jax.random.key(seed)
        x = -0.0002928 + 1 * jax.random.normal(jax.random.fold_in(_gk, 1), (4096, 256), jnp.float32)
        _a = jax.random.bernoulli(jax.random.fold_in(_gk, 2), 0.00195312, (4096, 4096))
        _a = jnp.logical_or(_a, jnp.swapaxes(_a, -1, -2))
        _a = jnp.logical_or(_a, jnp.eye(4096, dtype=bool))
        _af = _a.astype(jnp.float32)
        _af = _af * jax.random.uniform(jax.random.fold_in(_gk, 3), (4096, 4096), jnp.float32, 0.05, 5.41998)
        adj = _af
        return (x, adj)
    x, adj = _rec_inputs()

    def _L0_gnn_setup():
        import jax, jax.numpy as jnp
        import numpy as np
        N = 4096
        D = 256
        key = jax.random.key(seed)
        ks = jax.random.split(key, 6)
        s = 1.0 / np.sqrt(D)
        return {'x': jax.random.normal(ks[0], (N, D), jnp.float32), 'spatial_encoding': jax.random.normal(ks[1], (N, N), jnp.float32), 'edge_encoding': jax.random.normal(ks[2], (N, N), jnp.float32), 'Wq': jax.random.normal(ks[3], (D, D), jnp.float32) * s, 'bq': jnp.zeros((D,), jnp.float32), 'Wk': jax.random.normal(ks[4], (D, D), jnp.float32) * s, 'bk': jnp.zeros((D,), jnp.float32), 'Wv': jax.random.normal(ks[5], (D, D), jnp.float32) * s, 'bv': jnp.zeros((D,), jnp.float32)}
    _L0_gnn_all = _L0_gnn_setup()
    _L0_gnn_in = {k: v for k, v in _L0_gnn_all.items() if k in ('Wq', 'bq', 'Wk', 'bk', 'Wv', 'bv')}
    del _L0_gnn_all
    return {'x': x, 'adj': adj, 'L0_gnn_Wq': _L0_gnn_in['Wq'], 'L0_gnn_bq': _L0_gnn_in['bq'], 'L0_gnn_Wk': _L0_gnn_in['Wk'], 'L0_gnn_bk': _L0_gnn_in['bk'], 'L0_gnn_Wv': _L0_gnn_in['Wv'], 'L0_gnn_bv': _L0_gnn_in['bv']}

def reference(x, adj, L0_gnn_Wq, L0_gnn_bq, L0_gnn_Wk, L0_gnn_bk, L0_gnn_Wv, L0_gnn_bv):
    import jax
    import jax.numpy as jnp

    def _L0_gnn_ref(x, spatial_encoding, edge_encoding, Wq, bq, Wk, bk, Wv, bv):
        import jax, jax.numpy as jnp
        import numpy as np
        N = 4096
        D = 256
        q = x @ Wq.T + bq
        k = x @ Wk.T + bk
        v = x @ Wv.T + bv
        scale = 1.0 / jnp.sqrt(jnp.asarray(q.shape[-1], q.dtype))
        a = q @ k.T * scale + spatial_encoding + edge_encoding
        attn = jax.nn.softmax(a, axis=-1)
        return attn @ v
    h = jnp.maximum(_layernorm(x, axis=-1), 0.0)
    x = x + _L0_gnn_ref(h, adj, adj, L0_gnn_Wq, L0_gnn_bq, L0_gnn_Wk, L0_gnn_bk, L0_gnn_Wv, L0_gnn_bv)
    return x

_drawn_inputs = setup_inputs


def setup_inputs(seed=0):
    import zlib

    import numpy as np

    out = dict(_drawn_inputs(seed))
    spreads = {'L0_gnn_bq': (0.0, 0.675), 'L0_gnn_bk': (0.0, 0.8), 'L0_gnn_bv': (0.0, 0.1)}
    factors = {}
    for name, (base, spread) in spreads.items():
        noise = np.random.default_rng([zlib.crc32(name.encode()), seed]).standard_normal(out[name].shape)
        drawn = base * np.exp(spread * noise) if base else spread * noise
        out[name] = jnp.asarray(drawn.astype(out[name].dtype))
    for name, factor in factors.items():
        out[name] = (out[name] * factor).astype(out[name].dtype)
    return out
```

```python
import math

import concourse.bass as bass
from concourse import mybir
from contextlib import ExitStack

FP32 = mybir.dt.float32
FP16 = mybir.dt.float16
U32 = mybir.dt.uint32
ALU = mybir.AluOpType
ACT = mybir.ActivationFunctionType
AX = mybir.AxisListType

P = 128
N = 4096
D = 256
DC = D // P
TILES = N // P
CH = 512
CHUNKS = N // CH
KT = CH // P
SLOTS = TILES * CHUNKS
UNROLL = 2 * CHUNKS
GROUPS = CHUNKS
PIECE = 2 * CH
PIECES = N // PIECE

EPS = 1e-5
H_SCALE = 16.0
SCORE_SCALE = 1.0 / math.sqrt(D)
H_L1 = float(D)
G_TOP = 2.0 ** 14
V_TOP = 2.0 ** 13
LEAST_BOUND = 2.0 ** -20
LN_P_SCALE = 12 * math.log(2.0)

EXP_LAG = CHUNKS
T_LAG = EXP_LAG + 1
SPLIT_LAG = T_LAG + 1
V_LAG = SPLIT_LAG + 1
SCORE_BANKS = 4
T_BANKS = 2
W_RING = 4
SCALE_LEAD = 2
DRAIN = V_LAG


def attention_kernel(nc, x, adj, wq, bq, wk, bk, wv, bv, out):
    x_rows = x.rearrange("(t p) d -> p t d", p=P)
    out_rows = out.rearrange("(t p) d -> t p d", p=P)

    ctx = ExitStack()
    with ctx:
        def sb(name, shape, dt=FP32):
            return ctx.enter_context(nc.sbuf_tensor(name, shape, dt))

        def sem(name):
            return ctx.enter_context(nc.semaphore(name))

        rows = [sb(f"rows{b}", [P, N]) for b in range(2)]
        x_sb = sb("x_sb", [P, TILES, D])
        hT_hi = sb("hT_hi", [P, DC, N], FP16)
        hT_lo = sb("hT_lo", [P, DC, N], FP16)
        gT = sb("gT", [P, TILES, 2, DC, P], FP16)
        v_sb = sb("v_sb", [P, TILES, 2, D], FP16)
        g_tile = [sb(f"g_tile{b}", [P, 2, DC, P], FP16) for b in range(2)]
        wT_hi = sb("wT_hi", [P, W_RING, CH], FP16)
        wT_lo = sb("wT_lo", [P, W_RING, CH], FP16)
        h_grp = sb("h_grp", [P, KT, D])
        wq_sb = sb("wq_sb", [P, DC, D])
        wk_sb = sb("wk_sb", [P, DC, D])
        wv_sb = sb("wv_sb", [P, DC, D])
        bq_sb = sb("bq_sb", [P, DC])
        bk_sb = sb("bk_sb", [P, DC])
        bv_row = sb("bv_row", [P, D])
        bk_wide = sb("bk_wide", [P, DC, P])
        ones = sb("ones", [P, P])
        ident = sb("ident", [P, P])
        m_hi = sb("m_hi", [P, DC, D], FP16)
        m_lo = sb("m_lo", [P, DC, D], FP16)
        wvT_hi = sb("wvT_hi", [P, DC, D], FP16)
        wvT_lo = sb("wvT_lo", [P, DC, D], FP16)
        wqbk_row = sb("wqbk_row", [P, D])
        rbias0 = sb("rbias0", [P, 1])
        tops = sb("tops", [P, 3])
        all_tops = sb("all_tops", [P, 3])
        bound = sb("bound", [P, 2])
        power = sb("power", [P, 2])
        inv_power = sb("inv_power", [P, 2])
        m_scale = sb("m_scale", [P, 1])
        wv_scale = sb("wv_scale", [P, 1])
        kappa = sb("kappa", [P, 1])
        adj_scale = sb("adj_scale", [P, 1])
        exp_scale = sb("exp_scale", [P, 1])
        inv_omega = sb("inv_omega", [P, 1])
        g_bias = sb("g_bias", [P, DC])
        stats6 = sb("stats6", [P, KT, 6])
        mean_var = sb("mean_var", [P, 2, KT, 2])
        var_eps = sb("var_eps", [P, KT])
        minus_half = sb("minus_half", [P, KT])
        rstd = sb("rstd", [P, KT])
        ln_grp = sb("ln_grp", [P, 2, KT])
        ln_all = sb("ln_all", [P, GROUPS, 2, KT])
        ln_tile = [sb(f"ln_tile{b}", [P, 2]) for b in range(2)]
        h_tile = sb("h_tile", [P, D])
        r_scratch = sb("r_scratch", [P, D])
        r_row = sb("r_row", [P, 1])
        chunk_max = [sb(f"chunk_max{b}", [P, CHUNKS]) for b in range(2)]
        tile_max = sb("tile_max", [P, 1])
        row_max = sb("row_max", [P, 1])
        exp_bias = [sb(f"exp_bias{b}", [P, 1]) for b in range(2)]
        chunk_sum = [sb(f"chunk_sum{b}", [P, CHUNKS]) for b in range(2)]
        row_sum = sb("row_sum", [P, 1])
        inv_sum = sb("inv_sum", [P, 1])
        out_scale = sb("out_scale", [P, 1])
        x_bias = [sb(f"x_bias{b}", [P, D]) for b in range(2)]
        half_out = sb("half_out", [P, D])
        y = [sb(f"y{b}", [P, D]) for b in range(2)]

        bank = [ctx.enter_context(nc.psum_tensor(f"bank{b}", [P, CH], FP32)) for b in range(8)]
        score_ps = bank[0:SCORE_BANKS]
        t_ps = bank[4:4 + T_BANKS]
        o_ps = bank[6:8]
        hT_ps = bank[4:6]
        gT_ps = bank[0:2]
        v_ps = bank[2:4]
        m_ps = bank[6][:, :].rearrange("p (c d) -> p c d", c=DC)
        small_ps = bank[7]
        wvT_ps = bank[0][:, :].rearrange("p (c d) -> p c d", c=DC)

        wqk_loaded = sem("wqk_loaded")
        wv_loaded = sem("wv_loaded")
        bv_loaded = sem("bv_loaded")
        x_loaded = [sem(f"x_loaded{g}") for g in range(2)]
        adj_loaded = [sem(f"adj_loaded{q}") for q in range(PIECES)]
        stored = sem("stored")
        ones_set = sem("ones_set")
        ident_set = sem("ident_set")
        pool_step = sem("pool_step")
        bk_widened = sem("bk_widened")
        m_done = sem("m_done")
        small_done = sem("small_done")
        wvT_done = sem("wvT_done")
        tops_done = sem("tops_done")
        tops_shared = sem("tops_shared")
        scales_done = sem("scales_done")
        weights_hi = sem("weights_hi")
        weights_lo = sem("weights_lo")
        small_read = sem("small_read")
        stats_done = sem("stats_done")
        ln_done = sem("ln_done")
        h_done = sem("h_done")
        h_transposed = sem("h_transposed")
        hT_hi_done = sem("hT_hi_done")
        hT_lo_done = sem("hT_lo_done")
        g_projected = sem("g_projected")
        g_hi_done = sem("g_hi_done")
        g_lo_done = sem("g_lo_done")
        v_projected = sem("v_projected")
        v_hi_done = sem("v_hi_done")
        v_lo_done = sem("v_lo_done")
        dve_step = sem("dve_step")
        g_staged = sem("g_staged")
        xb_done = sem("xb_done")
        adj_scaled = sem("adj_scaled")
        scored = sem("scored")
        summed = sem("summed")
        bias_done = sem("bias_done")
        h_again = sem("h_again")
        r_done = sem("r_done")
        exped = sem("exped")
        transposed = sem("transposed")
        split_hi = sem("split_hi")
        split_lo = sem("split_lo")
        weighed = sem("weighed")
        y_done = sem("y_done")
        max_step = sem("max_step")
        fin_step = sem("fin_step")

        def wait(eng, s, value):
            if not isinstance(value, int) or value > 0:
                eng.wait_ge(s, value)

        def chunk_no(pair, j):
            return pair * UNROLL + j

        def tile_no(pair, j):
            return pair * 2 + j // CHUNKS

        def slots(eng, slot, peel_last=False):
            for j in range(UNROLL):
                slot(0, j, lambda lag, j=j: j >= lag)
            pairs = SLOTS // UNROLL
            with eng.Fori(1, pairs - peel_last) as pair:
                for j in range(UNROLL):
                    slot(pair, j, lambda lag: True)
            if peel_last:
                for j in range(UNROLL):
                    slot(pairs - 1, j, lambda lag: True)
            for j in range(DRAIN):
                slot(SLOTS // UNROLL, j, lambda lag, j=j: j < lag)

        block = ctx.enter_context(nc.Block())

        @block.sync
        def _(sp):
            def load_x(g):
                if g >= 2:
                    sp.wait_ge(x_loaded[g % 2], 16 * (g // 2))
                sp.dma_start(x_sb[:, g * KT:(g + 1) * KT, :],
                             x_rows[:, g * KT:(g + 1) * KT, :]).then_inc(x_loaded[g % 2], 16)

            load_x(0)
            for w_sb, w in ((wq_sb, wq), (wk_sb, wk)):
                sp.dma_start(w_sb[:], w.rearrange("(p c) d -> p c d", c=DC)
                             ).then_inc(wqk_loaded, 16)
            for b_sb, b in ((bq_sb, bq), (bk_sb, bk)):
                sp.dma_start(b_sb[:], b.rearrange("(p c) -> p c", c=DC)).then_inc(wqk_loaded, 16)
            load_x(1)
            sp.dma_start(wv_sb[:], wv.rearrange("(c p) d -> p c d", p=P)).then_inc(wv_loaded, 16)
            sp.dma_start(bv_row[:], bv.rearrange("(o d) -> o d", o=1).to_broadcast([P, D])
                         ).then_inc(bv_loaded, 16)
            for g in range(2, GROUPS):
                load_x(g)

            def tile_io(t, b, with_loads=True, stores=True):
                def known(value):
                    return value if isinstance(value, int) else sp.snap(value)

                row, stored_row = known(t * P), known((t - 3) * P)
                loads, stores_before, outputs = known(16 * t), known(16 * (t - 3)), known(t - 2)
                freed = [known(CHUNKS * (t - 2) + 2 * (q + 1)) for q in range(PIECES)]
                for q in range(PIECES):
                    if with_loads:
                        if q == 0:
                            wait(sp, adj_loaded[q], loads)
                        wait(sp, transposed, freed[q])
                        if q > 0:
                            wait(sp, adj_loaded[q], loads)
                        sp.dma_start(rows[b][:, q * PIECE:(q + 1) * PIECE],
                                     adj[bass.ds(row, P), q * PIECE:(q + 1) * PIECE]
                                     ).then_inc(adj_loaded[q], 16)
                    if q == 1 and stores:
                        wait(sp, stored, stores_before)
                        wait(sp, y_done, outputs)
                        sp.dma_start(out[bass.ds(stored_row, P), :], y[1 - b][:]
                                     ).then_inc(stored, 16)

            for t in range(4):
                tile_io(t, t % 2, stores=t >= 3)
            with sp.Fori(2, TILES // 2) as pair:
                for b in range(2):
                    tile_io(pair * 2 + b, b)
            for t in range(TILES, TILES + 3):
                tile_io(t, t % 2, with_loads=False)
            sp.wait_ge(stored, 16 * TILES)

        @block.gpsimd
        def _(pool):
            steps = [0]

            def link(ins):
                steps[0] += 1
                ins.then_inc(pool_step, 1)
                pool.wait_ge(pool_step, steps[0])

            nc.gpsimd.memset(ones[:], 1.0).then_inc(ones_set, 1)
            pool.wait_ge(ones_set, 1)
            nc.gpsimd.affine_select(out=ident[:], in_=ones[:], compare_op=ALU.is_equal, fill=0.0,
                                    base=0, pattern=[[-1, P]], channel_multiplier=1
                                    ).then_inc(ident_set, 1)
            link(nc.gpsimd.memset(minus_half[:], -0.5))

            def layernorm_factors(g):
                pool.wait_ge(stats_done, g + 1)
                if g >= 1:
                    pool.wait_ge(h_done, g)
                mv = mean_var[:, g % 2]
                link(nc.gpsimd.tensor_scalar(var_eps[:], mv[:, :, 1], EPS, None, ALU.add))
                link(nc.gpsimd.tensor_tensor(rstd[:], var_eps[:], minus_half[:], ALU.pow))
                link(nc.gpsimd.tensor_scalar(ln_grp[:, 0, :], rstd[:], H_SCALE, None, ALU.mult))
                link(nc.gpsimd.tensor_scalar(rstd[:], rstd[:], -H_SCALE, None, ALU.mult))
                link(nc.gpsimd.tensor_tensor(ln_grp[:, 1, :], rstd[:], mv[:, :, 0], ALU.mult))
                nc.gpsimd.tensor_copy(ln_all[:, g], ln_grp[:]).then_inc(ln_done, 1)

            layernorm_factors(0)
            layernorm_factors(1)
            pool.wait_ge(tops_done, 1)
            nc.gpsimd.partition_all_reduce(all_tops[:], tops[:], P, bass.bass_isa.ReduceOp.max
                                           ).then_inc(tops_shared, 1)
            for g in range(2, GROUPS):
                layernorm_factors(g)

            pool.wait_ge(ln_done, GROUPS)
            pool.wait_ge(bv_loaded, 16)
            for b in range(2):
                pool.wait_ge(x_loaded[b], 16 * GROUPS // 2)

            def stage(t, group, in_group, b, first):
                if first:
                    pool.wait_ge(g_lo_done, DC)
                wait(pool, scored, CHUNKS * (t - 1))
                nc.gpsimd.tensor_copy(
                    g_tile[b][:].rearrange("p s c q -> p (s c q)"),
                    gT[:, bass.ds(t, 1)].rearrange("p t s c q -> p (t s c q)"))
                wait(pool, h_again, t - 1)
                nc.gpsimd.tensor_copy(
                    ln_tile[b][:, :],
                    ln_all[:, bass.ds(group, 1), :, in_group].rearrange("p g s -> p (g s)")
                    ).then_inc(g_staged, 1)
                wait(pool, y_done, t - 1)
                wait(pool, stored, 16 * (t - 1))
                nc.gpsimd.tensor_tensor(
                    x_bias[b][:], x_sb[:, bass.ds(t, 1)].rearrange("p t d -> p (t d)"),
                    bv_row[:], ALU.add).then_inc(xb_done, 1)

            for t in range(KT):
                stage(t, 0, t, t % 2, True)
            pool.wait_ge(g_lo_done, DC * GROUPS)
            with pool.Fori(1, GROUPS) as i:
                for k in range(KT):
                    stage(i * KT + k, i, k, k % 2, False)

        @block.scalar
        def _(act):
            def normalise(g):
                act.wait_ge(ln_done, g + 1)
                act.wait_ge(x_loaded[g % 2], 16 * (g // 2 + 1))
                if g >= 1:
                    act.wait_ge(h_transposed, g)
                for k in range(KT):
                    last = nc.scalar.activation(h_grp[:, k, :], x_sb[:, g * KT + k, :], ACT.Relu,
                                                scale=ln_grp[:, 0, k:k + 1],
                                                bias=ln_grp[:, 1, k:k + 1])
                last.then_inc(h_done, 1)

            def split_h(g):
                act.wait_ge(h_transposed, g + 1)
                for c in range(DC):
                    nc.scalar.copy(hT_hi[:, c, g * CH:(g + 1) * CH], hT_ps[c][:]
                                   ).then_inc(hT_hi_done, 1)

            def split_g(g):
                for c in range(DC):
                    act.wait_ge(g_projected, DC * g + c + 1)
                    nc.scalar.activation(
                        gT[:, g * KT:(g + 1) * KT, 0, c, :],
                        gT_ps[c][:].rearrange("p (t q) -> p t q", t=KT), ACT.Identity,
                        bias=g_bias[:, c:c + 1]).then_inc(g_hi_done, 1)

            def split_v(g):
                for u in range(2):
                    act.wait_ge(v_projected, 2 * g + u + 1)
                    nc.scalar.copy(v_sb[:, g * KT + 2 * u:g * KT + 2 * u + 2, 0, :],
                                   v_ps[u][:].rearrange("p (t d) -> p t d", t=2)
                                   ).then_inc(v_hi_done, 1)

            normalise(0)
            split_h(0)
            normalise(1)
            act.wait_ge(scales_done, 1)
            nc.scalar.activation(m_hi[:], m_ps, ACT.Copy, scale=m_scale[:]).then_inc(weights_hi, 1)
            nc.scalar.activation(wvT_hi[:], wvT_ps, ACT.Copy, scale=wv_scale[:]
                                 ).then_inc(weights_hi, 1)
            for g in range(GROUPS):
                if g + 1 < GROUPS:
                    split_h(g + 1)
                if g + 2 < GROUPS:
                    normalise(g + 2)
                split_g(g)
                split_v(g)

            def scaled_ahead(pair, j):
                return not isinstance(pair, int) or chunk_no(pair, j) + SCALE_LEAD < SLOTS

            def scale_adj(pair, m):
                q, b = m % CHUNKS // 2, m // CHUNKS % 2
                act.wait_ge(adj_loaded[q], 16 * (tile_no(pair, m) + 1))
                piece = rows[b][:, q * PIECE:(q + 1) * PIECE]
                nc.scalar.activation(piece, piece, ACT.Copy, scale=adj_scale[:]
                                     ).then_inc(adj_scaled, 1)

            for m in range(0, SCALE_LEAD, 2):
                scale_adj(0, m)

            def slot(pair, j, runs):
                c = j % CHUNKS
                tile = tile_no(pair, j)
                b = j // CHUNKS % 2
                if runs(EXP_LAG):
                    if c == 0:
                        act.wait_ge(bias_done, tile)
                    w = rows[1 - b][:, c * CH:(c + 1) * CH]
                    nc.scalar.activation(w, w, ACT.Exp, scale=exp_scale[:], bias=exp_bias[1 - b][:],
                                         accum_out=chunk_sum[1 - b][:, c:c + 1]
                                         ).then_inc(exped, 1)
                if runs(T_LAG):
                    m, at = chunk_no(pair, j - T_LAG), j - T_LAG
                    wait(act, weighed, m - W_RING + 1)
                    act.wait_ge(transposed, m + 1)
                    nc.scalar.copy(wT_hi[:, at % W_RING, :], t_ps[at % T_BANKS][:]
                                   ).then_inc(split_hi, 1)
                if j % 2 == 0 and scaled_ahead(pair, j):
                    scale_adj(pair, j + SCALE_LEAD)
                if c == 2 and runs(0):
                    act.wait_ge(g_staged, tile + 1)
                    wait(act, r_done, tile)
                    nc.scalar.activation(h_tile[:],
                                         x_sb[:, bass.ds(tile, 1)].rearrange("p t d -> p (t d)"),
                                         ACT.Relu, scale=ln_tile[b][:, 0:1],
                                         bias=ln_tile[b][:, 1:2]).then_inc(h_again, 1)

            slots(act, slot, peel_last=True)

        @block.vector
        def _(dve):
            steps = [0]

            def link(ins):
                steps[0] += 1
                ins.then_inc(dve_step, 1)
                dve.wait_ge(dve_step, steps[0])

            def statistics(g):
                dve.wait_ge(x_loaded[g % 2], 16 * (g // 2 + 1))
                wait(dve, stats_done, g)
                wait(dve, ln_done, g - 1)
                for k in range(KT):
                    last = nc.vector.bn_stats(stats6[:, k, :], x_sb[:, g * KT + k, :])
                link(last)
                for k in range(KT):
                    last = nc.vector.bn_aggr(mean_var[:, g % 2, k, :], stats6[:, k, :])
                last.then_inc(stats_done, 1)

            def split_h(g):
                for c in range(DC):
                    dve.wait_ge(hT_hi_done, DC * g + c + 1)
                    nc.vector.tensor_tensor(hT_lo[:, c, g * CH:(g + 1) * CH], hT_ps[c][:],
                                            hT_hi[:, c, g * CH:(g + 1) * CH], ALU.subtract
                                            ).then_inc(hT_lo_done, 1)

            def split_g(g):
                for c in range(DC):
                    dve.wait_ge(g_hi_done, DC * g + c + 1)
                    nc.vector.scalar_tensor_tensor(
                        gT[:, g * KT:(g + 1) * KT, 1, c, :],
                        gT_ps[c][:].rearrange("p (t q) -> p t q", t=KT), g_bias[:, c:c + 1],
                        gT[:, g * KT:(g + 1) * KT, 0, c, :], ALU.add, ALU.subtract
                        ).then_inc(g_lo_done, 1)

            def split_v(g):
                for u in range(2):
                    dve.wait_ge(v_hi_done, 2 * g + u + 1)
                    pair = v_sb[:, g * KT + 2 * u:g * KT + 2 * u + 2]
                    nc.vector.tensor_tensor(pair[:, :, 1, :],
                                            v_ps[u][:].rearrange("p (t d) -> p t d", t=2),
                                            pair[:, :, 0, :], ALU.subtract).then_inc(v_lo_done, 1)

            dve.wait_ge(wqk_loaded, 64)
            dve.wait_ge(ones_set, 1)
            for c in range(DC):
                last = nc.vector.tensor_scalar(bk_wide[:, c, :], ones[:], bk_sb[:, c:c + 1], None,
                                               ALU.mult)
            last.then_inc(bk_widened, 1)
            statistics(0)
            statistics(1)

            dve.wait_ge(m_done, 1)
            nc.vector.tensor_reduce(tops[:, 0:1], bank[6][:], AX.X, ALU.max,
                                    apply_absolute_value=True)
            dve.wait_ge(small_done, 1)
            nc.vector.tensor_reduce(tops[:, 1:2], small_ps[:, D:D + DC], AX.X, ALU.max,
                                    apply_absolute_value=True)
            nc.vector.tensor_copy(wqbk_row[:], small_ps[:, 0:D])
            nc.vector.tensor_scalar(rbias0[:], small_ps[:, D + DC:D + DC + 1], SCORE_SCALE, None,
                                    ALU.mult)
            dve.wait_ge(wvT_done, 1)
            nc.vector.tensor_reduce(tops[:, 2:3], bank[0][:], AX.X, ALU.max,
                                    apply_absolute_value=True).then_inc(tops_done, 1)
            dve.wait_ge(tops_shared, 1)
            link(nc.vector.scalar_tensor_tensor(bound[:, 0:1], all_tops[:, 0:1], H_L1,
                                                all_tops[:, 1:2], ALU.mult, ALU.add))
            link(nc.vector.tensor_scalar(bound[:, 1:2], all_tops[:, 2:3], H_L1, None, ALU.mult))
            link(nc.vector.tensor_scalar(bound[:], bound[:], LEAST_BOUND, None, ALU.max))
            link(nc.vector.tensor_scalar(power[:].bitcast(U32), bound[:].bitcast(U32), 0x7F800000,
                                         None, ALU.bitwise_and))
            link(nc.vector.reciprocal(inv_power[:], power[:]))
            nc.vector.tensor_scalar(kappa[:], inv_power[:, 0:1], G_TOP, None, ALU.mult)
            nc.vector.tensor_scalar(m_scale[:], inv_power[:, 0:1], G_TOP / H_SCALE, None, ALU.mult)
            nc.vector.tensor_scalar(wv_scale[:], inv_power[:, 1:2], V_TOP / H_SCALE, None, ALU.mult)
            nc.vector.tensor_scalar(adj_scale[:], inv_power[:, 0:1],
                                    2 * G_TOP * H_SCALE / SCORE_SCALE, None, ALU.mult)
            nc.vector.tensor_scalar(exp_scale[:], power[:, 0:1], SCORE_SCALE / (G_TOP * H_SCALE),
                                    None, ALU.mult)
            link(nc.vector.tensor_scalar(inv_omega[:], power[:, 1:2], 1.0 / V_TOP, None, ALU.mult))
            nc.vector.tensor_scalar(g_bias[:], small_ps[:, D:D + DC], kappa[:], None, ALU.mult
                                    ).then_inc(scales_done, 1)
            dve.wait_ge(weights_hi, 2)
            nc.vector.scalar_tensor_tensor(m_lo[:].rearrange("p c d -> p (c d)"), bank[6][:],
                                           m_scale[:], m_hi[:].rearrange("p c d -> p (c d)"),
                                           ALU.mult, ALU.subtract)
            nc.vector.scalar_tensor_tensor(wvT_lo[:].rearrange("p c d -> p (c d)"), bank[0][:],
                                           wv_scale[:], wvT_hi[:].rearrange("p c d -> p (c d)"),
                                           ALU.mult, ALU.subtract).then_inc(weights_lo, 1)
            split_h(0)
            for g in range(GROUPS):
                if g + 2 < GROUPS:
                    statistics(g + 2)
                if g + 1 < GROUPS:
                    split_h(g + 1)
                split_g(g)
                split_v(g)

            def slot(pair, j, runs):
                c = j % CHUNKS
                tile = tile_no(pair, j)
                b = j // CHUNKS % 2
                if runs(0):
                    dve.wait_ge(adj_scaled, pair * (UNROLL // 2) + j // 2 + 1)
                    dve.wait_ge(scored, chunk_no(pair, j) + 1)
                if runs(SPLIT_LAG):
                    m, at = chunk_no(pair, j - SPLIT_LAG), j - SPLIT_LAG
                    dve.wait_ge(split_hi, m + 1)
                    wait(dve, weighed, m - W_RING + 1)
                    nc.vector.tensor_tensor(wT_lo[:, at % W_RING, :], t_ps[at % T_BANKS][:],
                                            wT_hi[:, at % W_RING, :], ALU.subtract
                                            ).then_inc(split_lo, 1)
                if runs(0):
                    a = rows[b][:, c * CH:(c + 1) * CH]
                    nc.vector.tensor_tensor_reduce(
                        out=a, in0=score_ps[j % SCORE_BANKS][:], in1=a, scale=1.0,
                        scalar=-3.0e38, op0=ALU.add, op1=ALU.max,
                        accum_out=chunk_max[b][:, c:c + 1]).then_inc(summed, 1)
                    if c == 4:
                        dve.wait_ge(h_again, tile + 1)
                        nc.vector.tensor_tensor_reduce(
                            out=r_scratch[:], in0=h_tile[:], in1=wqbk_row[:],
                            scale=SCORE_SCALE / H_SCALE, scalar=rbias0[:], op0=ALU.mult,
                            op1=ALU.add, accum_out=r_row[:]).then_inc(r_done, 1)
                    if c == CHUNKS - 1:
                        dve.wait_ge(summed, chunk_no(pair, j) + 1)
                        nc.vector.reduce_max(tile_max[:], chunk_max[b][:], AX.X
                                             ).then_inc(max_step, 1)
                        dve.wait_ge(max_step, tile * 2 + 1)
                        dve.wait_ge(r_done, tile + 1)
                        nc.vector.scalar_tensor_tensor(row_max[:], tile_max[:], exp_scale[:],
                                                       r_row[:], ALU.mult, ALU.add
                                                       ).then_inc(max_step, 1)
                        dve.wait_ge(max_step, tile * 2 + 2)
                        wait(dve, exped, CHUNKS * (tile - 1))
                        nc.vector.scalar_tensor_tensor(exp_bias[b][:], r_row[:], LN_P_SCALE,
                                                       row_max[:], ALU.add, ALU.subtract
                                                       ).then_inc(bias_done, 1)
                        dve.wait_ge(bias_done, tile + 1)
                if c == 3 and runs(2 * CHUNKS + 3):
                    finish(tile - 2, b)

            def finish(t, parity):
                dve.wait_ge(exped, CHUNKS * (t + 1))
                nc.vector.reduce_sum(row_sum[:], chunk_sum[parity][:], AX.X).then_inc(fin_step, 1)
                dve.wait_ge(fin_step, t * 4 + 1)
                nc.vector.reciprocal(inv_sum[:], row_sum[:]).then_inc(fin_step, 1)
                dve.wait_ge(fin_step, 4 * t + 2)
                nc.vector.tensor_tensor(out_scale[:], inv_sum[:], inv_omega[:], ALU.mult
                                        ).then_inc(fin_step, 1)
                dve.wait_ge(fin_step, 4 * t + 3)
                dve.wait_ge(weighed, CHUNKS * (t + 1))
                dve.wait_ge(xb_done, t + 1)
                nc.vector.scalar_tensor_tensor(half_out[:], o_ps[parity][:, D:2 * D], out_scale[:],
                                               x_bias[parity][:], ALU.mult, ALU.add
                                               ).then_inc(fin_step, 1)
                dve.wait_ge(fin_step, 4 * t + 4)
                nc.vector.scalar_tensor_tensor(y[parity][:], o_ps[parity][:, 0:D], out_scale[:],
                                               half_out[:], ALU.mult, ALU.add
                                               ).then_inc(y_done, 1)
                dve.wait_ge(y_done, t + 1)

            slots(dve, slot)
            finish(TILES - 1, (TILES - 1) % 2)

        @block.tensor
        def _(pe):
            def matmul(out_ap, stationary, moving, first, last):
                return nc.tensor.matmul(out_ap, stationary, moving, start=first, stop=last)

            pe.wait_ge(wqk_loaded, 64)
            for c in range(DC):
                for e in range(DC):
                    last = matmul(m_ps[:, c, :], wq_sb[:, e, c * P:(c + 1) * P], wk_sb[:, e, :],
                                  e == 0, e == DC - 1)
            last.then_inc(m_done, 1)
            for c in range(DC):
                for e in range(DC):
                    matmul(small_ps[:, D + c:D + c + 1], wk_sb[:, e, c * P:(c + 1) * P],
                           bq_sb[:, e:e + 1], e == 0, e == DC - 1)
            pe.wait_ge(bk_widened, 1)
            for e in range(DC):
                matmul(small_ps[:, 0:D], bk_wide[:, e, :], wq_sb[:, e, :], e == 0, e == DC - 1)
            for e in range(DC):
                last = matmul(small_ps[:, D + DC:D + DC + 1], bk_wide[:, e, :], bq_sb[:, e:e + 1],
                              e == 0, e == DC - 1)
            last.then_inc(small_done, 1)
            pe.wait_ge(wv_loaded, 16)
            pe.wait_ge(ident_set, 1)
            for c in range(DC):
                for e in range(DC):
                    last = nc.tensor.transpose(wvT_ps[:, c, e * P:(e + 1) * P],
                                               wv_sb[:, e, c * P:(c + 1) * P], ident[:])
            last.then_inc(wvT_done, 1)

            def transpose_h(g):
                pe.wait_ge(h_done, g + 1)
                if g >= 1:
                    pe.wait_ge(hT_lo_done, DC * g)
                for c in range(DC):
                    for k in range(KT):
                        last = nc.tensor.transpose(hT_ps[c][:, k * P:(k + 1) * P],
                                                   h_grp[:, k, c * P:(c + 1) * P], ident[:])
                last.then_inc(h_transposed, 1)

            def three_products(out_ap, parts):
                for i, (a_hi, a_lo, b_hi, b_lo) in enumerate(parts):
                    matmul(out_ap, a_hi, b_hi, i == 0, False)
                    matmul(out_ap, a_hi, b_lo, False, False)
                    last = matmul(out_ap, a_lo, b_hi, False, i == len(parts) - 1)
                return last

            def project(g):
                pe.wait_ge(hT_lo_done, DC * (g + 1))
                keys = slice(g * CH, (g + 1) * CH)
                for c in range(DC):
                    cols = slice(c * P, (c + 1) * P)
                    wait(pe, g_lo_done, DC * (g - 1) + c + 1)
                    three_products(gT_ps[c][:],
                                   [(m_hi[:, k, cols], m_lo[:, k, cols],
                                     hT_hi[:, k, keys], hT_lo[:, k, keys]) for k in range(DC)]
                                   ).then_inc(g_projected, 1)
                for u in range(2):
                    wait(pe, v_lo_done, 2 * (g - 1) + u + 1)
                    for w in range(2):
                        k0 = g * CH + (2 * u + w) * P
                        last = three_products(
                            v_ps[u][:, w * D:(w + 1) * D],
                            [(hT_hi[:, k, k0:k0 + P], hT_lo[:, k, k0:k0 + P],
                              wvT_hi[:, k, :], wvT_lo[:, k, :]) for k in range(DC)])
                    last.then_inc(v_projected, 1)

            transpose_h(0)
            pe.wait_ge(weights_lo, 1)
            for g in range(GROUPS):
                if g + 1 < GROUPS:
                    transpose_h(g + 1)
                project(g)
            pe.wait_ge(g_lo_done, DC * GROUPS)
            pe.wait_ge(v_lo_done, 2 * GROUPS)

            def score(pair, j):
                c = j % CHUNKS
                b = j // CHUNKS % 2
                tile = tile_no(pair, j)
                if c == 0:
                    pe.wait_ge(g_staged, tile + 1)
                wait(pe, summed, chunk_no(pair, j) - SCORE_BANKS + 1)
                keys = slice(c * CH, (c + 1) * CH)
                g = g_tile[b]
                three_products(score_ps[j % SCORE_BANKS][:],
                               [(g[:, 0, k, :], g[:, 1, k, :], hT_hi[:, k, keys],
                                 hT_lo[:, k, keys]) for k in range(DC)]).then_inc(scored, 1)

            def transpose_weights(pair, j):
                m = chunk_no(pair, j)
                c, b = j % CHUNKS, j // CHUNKS % 2
                pe.wait_ge(exped, m + 1)
                wait(pe, split_lo, m - T_BANKS + 1)
                for k in range(KT):
                    at = c * CH + k * P
                    last = nc.tensor.transpose(t_ps[j % T_BANKS][:, k * P:(k + 1) * P],
                                               rows[b][:, at:at + P], ident[:])
                last.then_inc(transposed, 1)

            def weigh(pair, j):
                c, b, at = j % CHUNKS, j // CHUNKS % 2, j % W_RING
                pe.wait_ge(split_lo, chunk_no(pair, j) + 1)
                for k in range(KT):
                    kt = c * KT + k
                    matmul(o_ps[b][:], wT_hi[:, at, k * P:(k + 1) * P],
                           v_sb[:, kt].rearrange("p s d -> p (s d)"), kt == 0, False)
                    last = matmul(o_ps[b][:, 0:D], wT_lo[:, at, k * P:(k + 1) * P],
                                  v_sb[:, kt, 0, :], False, kt == CHUNKS * KT - 1)
                last.then_inc(weighed, 1)

            def slot(pair, j, runs):
                if runs(0):
                    score(pair, j)
                if runs(T_LAG):
                    transpose_weights(pair, j - T_LAG)
                if runs(V_LAG):
                    weigh(pair, j - V_LAG)

            slots(pe, slot)


_INS = ['x', 'adj', 'L0_gnn_Wq', 'L0_gnn_bq', 'L0_gnn_Wk', 'L0_gnn_bk', 'L0_gnn_Wv', 'L0_gnn_bv']


def kernel(**inputs):
    import numpy as _np
    import concourse.bacc as _bacc
    from concourse.bass_utils import run_bass_kernel_spmd as _run

    nc = _bacc.Bacc("TRN2", target_bir_lowering=False, num_devices=1)
    arrays, args = {}, []
    for name in _INS:
        a = _np.ascontiguousarray(inputs[name])
        arrays[f"in_{name}"] = a
        args.append(nc.dram_tensor(f"in_{name}", a.shape, mybir.dt.from_np(a.dtype),
                                   kind="ExternalInput").ap())
    result = nc.dram_tensor("out_y", (N, D), FP32, kind="ExternalOutput").ap()
    attention_kernel(nc, *args, result)
    r = _run(nc, [arrays], core_ids=[0])
    return r.results[0]["out_y"]
```

```python
import math

import concourse.bass as bass
from concourse import mybir
from contextlib import ExitStack

FP32 = mybir.dt.float32
FP16 = mybir.dt.float16
U32 = mybir.dt.uint32
ALU = mybir.AluOpType
ACT = mybir.ActivationFunctionType
AX = mybir.AxisListType

P = 128
N = 4096
D = 256
DC = D // P
TILES = N // P
CH = 512
CHUNKS = N // CH
KT = CH // P
SLOTS = TILES * CHUNKS
UNROLL = 2 * CHUNKS
GROUPS = CHUNKS
PIECE = 2 * CH
PIECES = N // PIECE

EPS = 1e-5
H_SCALE = 16.0
SCORE_SCALE = 1.0 / math.sqrt(D)
H_L1 = float(D)
G_TOP = 2.0 ** 14
V_TOP = 2.0 ** 13
LEAST_BOUND = 2.0 ** -20
LN_P_SCALE = 12 * math.log(2.0)

EXP_LAG = CHUNKS
HI_LAG = EXP_LAG + 1
LO_LAG = HI_LAG + 1
TR_LAG = LO_LAG + 1
V_LAG = TR_LAG + 3
SCORE_BANKS = 4
SPLIT_RING = 4
W_RING = 4
SCALE_LEAD = 2
FINISH_AT = V_LAG - CHUNKS
DRAIN = V_LAG


def attention_kernel(nc, x, adj, wq, bq, wk, bk, wv, bv, out):
    x_rows = x.rearrange("(t p) d -> p t d", p=P)
    out_rows = out.rearrange("(t p) d -> t p d", p=P)

    ctx = ExitStack()
    with ctx:
        def sb(name, shape, dt=FP32):
            return ctx.enter_context(nc.sbuf_tensor(name, shape, dt))

        def sem(name):
            return ctx.enter_context(nc.semaphore(name))

        rows = [sb(f"rows{b}", [P, N]) for b in range(2)]
        x_sb = sb("x_sb", [P, TILES, D])
        hT_hi = sb("hT_hi", [P, DC, N], FP16)
        hT_lo = sb("hT_lo", [P, DC, N], FP16)
        gT = sb("gT", [P, TILES, 2, DC, P], FP16)
        v_sb = sb("v_sb", [P, TILES, 2, D], FP16)
        g_tile = [sb(f"g_tile{b}", [P, 2, DC, P], FP16) for b in range(2)]
        w_split = sb("w_split", [P, SPLIT_RING, 2, CH], FP16)
        wT = sb("wT", [P, W_RING, 2 * KT, P], FP16)
        h_grp = sb("h_grp", [P, 2, KT, D])
        wq_sb = sb("wq_sb", [P, DC, D])
        wk_sb = sb("wk_sb", [P, DC, D])
        wv_sb = sb("wv_sb", [P, DC, D])
        bq_sb = sb("bq_sb", [P, DC])
        bk_sb = sb("bk_sb", [P, DC])
        bv_row = sb("bv_row", [P, D])
        bk_wide = sb("bk_wide", [P, DC, P])
        ones = sb("ones", [P, P])
        ident = sb("ident", [P, P])
        m_hi = sb("m_hi", [P, DC, D], FP16)
        m_lo = sb("m_lo", [P, DC, D], FP16)
        wvT_hi = sb("wvT_hi", [P, DC, D], FP16)
        wvT_lo = sb("wvT_lo", [P, DC, D], FP16)
        wqbk_row = sb("wqbk_row", [P, D])
        rbias0 = sb("rbias0", [P, 1])
        tops = sb("tops", [P, 3])
        all_tops = sb("all_tops", [P, 3])
        bound = sb("bound", [P, 2])
        power = sb("power", [P, 2])
        inv_power = sb("inv_power", [P, 2])
        m_scale = sb("m_scale", [P, 1])
        wv_scale = sb("wv_scale", [P, 1])
        kappa = sb("kappa", [P, 1])
        adj_scale = sb("adj_scale", [P, 1])
        exp_scale = sb("exp_scale", [P, 1])
        inv_omega = sb("inv_omega", [P, 1])
        g_bias = sb("g_bias", [P, DC])
        stats6 = sb("stats6", [P, KT, 6])
        mean_var = sb("mean_var", [P, KT, 2])
        var_eps = sb("var_eps", [P, 2, KT])
        neg_mean = sb("neg_mean", [P, 2, KT])
        minus_half = sb("minus_half", [P, KT])
        ln_all = sb("ln_all", [P, GROUPS, 2, KT])
        ln_tile = [sb(f"ln_tile{b}", [P, 2]) for b in range(2)]
        h_tile = sb("h_tile", [P, D])
        r_row = sb("r_row", [P, 1])
        chunk_max = [sb(f"chunk_max{b}", [P, CHUNKS]) for b in range(2)]
        tile_max = sb("tile_max", [P, 1])
        row_max = sb("row_max", [P, 1])
        exp_bias = [sb(f"exp_bias{b}", [P, 1]) for b in range(2)]
        chunk_sum = [sb(f"chunk_sum{b}", [P, CHUNKS]) for b in range(2)]
        row_sum = sb("row_sum", [P, 1])
        inv_sum = sb("inv_sum", [P, 1])
        out_scale = sb("out_scale", [P, 1])
        x_bias = [sb(f"x_bias{b}", [P, D]) for b in range(2)]
        half_out = sb("half_out", [P, D])
        y = [sb(f"y{b}", [P, D]) for b in range(2)]

        bank = [ctx.enter_context(nc.psum_tensor(f"bank{b}", [P, CH], FP32)) for b in range(8)]
        score_ps = bank[0:SCORE_BANKS]
        o_ps = bank[6:8]
        hT_ps = bank[4:6]
        gT_ps = bank[0:2]
        v_ps = bank[2:4]
        m_ps = bank[6][:, :].rearrange("p (c d) -> p c d", c=DC)
        small_ps = bank[7]
        wvT_ps = bank[0][:, :].rearrange("p (c d) -> p c d", c=DC)

        wqk_loaded = sem("wqk_loaded")
        wv_loaded = sem("wv_loaded")
        bv_loaded = sem("bv_loaded")
        x_loaded = [sem(f"x_loaded{g}") for g in range(2)]
        adj_loaded = [sem(f"adj_loaded{q}") for q in range(PIECES)]
        stored = sem("stored")
        ones_set = sem("ones_set")
        ident_set = sem("ident_set")
        pool_step = sem("pool_step")
        bk_widened = sem("bk_widened")
        m_done = sem("m_done")
        small_done = sem("small_done")
        wvT_done = sem("wvT_done")
        tops_done = sem("tops_done")
        tops_shared = sem("tops_shared")
        scales_done = sem("scales_done")
        weights_hi = sem("weights_hi")
        weights_lo = sem("weights_lo")
        small_read = sem("small_read")
        stats_done = sem("stats_done")
        ln_done = sem("ln_done")
        h_done = sem("h_done")
        h_transposed = sem("h_transposed")
        hT_hi_done = sem("hT_hi_done")
        hT_lo_done = sem("hT_lo_done")
        g_projected = sem("g_projected")
        g_hi_done = sem("g_hi_done")
        g_lo_done = sem("g_lo_done")
        v_projected = sem("v_projected")
        v_hi_done = sem("v_hi_done")
        v_lo_done = sem("v_lo_done")
        dve_step = sem("dve_step")
        g_staged = sem("g_staged")
        xb_done = sem("xb_done")
        adj_scaled = sem("adj_scaled")
        scored = sem("scored")
        summed = sem("summed")
        bias_done = sem("bias_done")
        h_again = sem("h_again")
        r_done = sem("r_done")
        exped = sem("exped")
        transposed = [sem(f"transposed{b}") for b in range(2)]
        split_hi = sem("split_hi")
        split_lo = sem("split_lo")
        weighed = sem("weighed")
        y_done = sem("y_done")
        transpose_released = sem("transpose_released")
        max_step = sem("max_step")
        fin_step = sem("fin_step")

        def wait(eng, s, value):
            if not isinstance(value, int) or value > 0:
                eng.wait_ge(s, value)

        def chunk_no(pair, j):
            return pair * UNROLL + j

        def tile_no(pair, j):
            return pair * 2 + j // CHUNKS

        def slots(eng, slot, peel_last=False):
            for j in range(UNROLL):
                slot(0, j, lambda lag, j=j: j >= lag)
            pairs = SLOTS // UNROLL
            with eng.Fori(1, pairs - peel_last) as pair:
                for j in range(UNROLL):
                    slot(pair, j, lambda lag: True)
            if peel_last:
                for j in range(UNROLL):
                    slot(pairs - 1, j, lambda lag: True)
            for j in range(DRAIN):
                slot(SLOTS // UNROLL, j, lambda lag, j=j: j < lag)

        block = ctx.enter_context(nc.Block())

        @block.sync
        def _(sp):
            def load_x(g):
                if g >= 2:
                    sp.wait_ge(x_loaded[g % 2], 16 * (g // 2))
                sp.dma_start(x_sb[:, g * KT:(g + 1) * KT, :],
                             x_rows[:, g * KT:(g + 1) * KT, :]).then_inc(x_loaded[g % 2], 16)

            load_x(0)
            for w_sb, w in ((wq_sb, wq), (wk_sb, wk)):
                sp.dma_start(w_sb[:], w.rearrange("(p c) d -> p c d", c=DC)
                             ).then_inc(wqk_loaded, 16)
            for b_sb, b in ((bq_sb, bq), (bk_sb, bk)):
                sp.dma_start(b_sb[:], b.rearrange("(p c) -> p c", c=DC)).then_inc(wqk_loaded, 16)
            load_x(1)
            sp.dma_start(wv_sb[:], wv.rearrange("(c p) d -> p c d", p=P)).then_inc(wv_loaded, 16)
            sp.dma_start(bv_row[:], bv.rearrange("(o d) -> o d", o=1).to_broadcast([P, D])
                         ).then_inc(bv_loaded, 16)
            for g in range(2, GROUPS):
                load_x(g)

            def tile_io(t, b, with_loads=True, stores=True):
                def known(value):
                    return value if isinstance(value, int) else sp.snap(value)

                row, stored_row = known(t * P), known((t - 3) * P)
                loads, stores_before, outputs = known(16 * t), known(16 * (t - 3)), known(t - 2)
                freed = [known(CHUNKS * (t - 2) + 2 * (q + 1)) for q in range(PIECES)]
                for q in range(PIECES):
                    if with_loads:
                        if q == 0:
                            wait(sp, adj_loaded[q], loads)
                        wait(sp, split_lo, freed[q])
                        if q > 0:
                            wait(sp, adj_loaded[q], loads)
                        sp.dma_start(rows[b][:, q * PIECE:(q + 1) * PIECE],
                                     adj[bass.ds(row, P), q * PIECE:(q + 1) * PIECE]
                                     ).then_inc(adj_loaded[q], 16)
                    if q == 1 and stores:
                        wait(sp, stored, stores_before)
                        wait(sp, y_done, outputs)
                        sp.dma_start(out[bass.ds(stored_row, P), :], y[1 - b][:]
                                     ).then_inc(stored, 16)

            for t in range(4):
                tile_io(t, t % 2, stores=t >= 3)
            with sp.Fori(2, TILES // 2) as pair:
                for b in range(2):
                    tile_io(pair * 2 + b, b)
            for t in range(TILES, TILES + 3):
                tile_io(t, t % 2, with_loads=False)
            sp.wait_ge(stored, 16 * TILES)

        @block.gpsimd
        def _(pool):
            steps = [0]

            def link(ins):
                steps[0] += 1
                ins.then_inc(pool_step, 1)
                pool.wait_ge(pool_step, steps[0])

            nc.gpsimd.memset(ones[:], 1.0).then_inc(ones_set, 1)
            pool.wait_ge(ones_set, 1)
            nc.gpsimd.affine_select(out=ident[:], in_=ones[:], compare_op=ALU.is_equal, fill=0.0,
                                    base=0, pattern=[[-1, P]], channel_multiplier=1
                                    ).then_inc(ident_set, 1)
            link(nc.gpsimd.memset(minus_half[:], -0.5))

            def layernorm_factors(g):
                pool.wait_ge(stats_done, g + 1)
                scale, bias = ln_all[:, g, 0, :], ln_all[:, g, 1, :]
                link(nc.gpsimd.tensor_tensor(scale, var_eps[:, g % 2], minus_half[:], ALU.pow))
                nc.gpsimd.tensor_tensor(bias, scale, neg_mean[:, g % 2], ALU.mult
                                        ).then_inc(ln_done, 1)

            layernorm_factors(0)
            layernorm_factors(1)
            layernorm_factors(2)
            pool.wait_ge(tops_done, 1)
            nc.gpsimd.partition_all_reduce(all_tops[:], tops[:], P, bass.bass_isa.ReduceOp.max
                                           ).then_inc(tops_shared, 1)
            for g in range(3, GROUPS):
                layernorm_factors(g)

            pool.wait_ge(ln_done, GROUPS)
            pool.wait_ge(bv_loaded, 16)
            for b in range(2):
                pool.wait_ge(x_loaded[b], 16 * GROUPS // 2)

            def stage(t, group, in_group, b, first):
                if first:
                    pool.wait_ge(g_lo_done, DC)
                wait(pool, scored, CHUNKS * (t - 1))
                nc.gpsimd.tensor_copy(
                    g_tile[b][:].rearrange("p s c q -> p (s c q)"),
                    gT[:, bass.ds(t, 1)].rearrange("p t s c q -> p (t s c q)"))
                wait(pool, h_again, t - 1)
                nc.gpsimd.tensor_copy(
                    ln_tile[b][:, :],
                    ln_all[:, bass.ds(group, 1), :, in_group].rearrange("p g s -> p (g s)")
                    ).then_inc(g_staged, 1)

            def add_bias(t, b):
                wait(pool, y_done, t - 1)
                wait(pool, stored, 16 * (t - 1))
                nc.gpsimd.tensor_tensor(
                    x_bias[b][:], x_sb[:, bass.ds(t, 1)].rearrange("p t d -> p (t d)"),
                    bv_row[:], ALU.add).then_inc(xb_done, 1)

            for t in range(KT):
                stage(t, 0, t, t % 2, True)
                if t >= 1:
                    add_bias(t - 1, (t - 1) % 2)
            pool.wait_ge(g_lo_done, DC * GROUPS)
            with pool.Fori(1, GROUPS) as i:
                for k in range(KT):
                    stage(i * KT + k, i, k, k % 2, False)
                    add_bias(i * KT + (k - 1), (k - 1) % 2)
            add_bias(TILES - 1, (TILES - 1) % 2)

        @block.scalar
        def _(act):
            def normalise(g):
                act.wait_ge(ln_done, g + 1)
                act.wait_ge(x_loaded[g % 2], 16 * (g // 2 + 1))
                wait(act, h_transposed, g - 1)
                for k in range(KT):
                    last = nc.scalar.activation(h_grp[:, g % 2, k, :], x_sb[:, g * KT + k, :], ACT.Relu,
                                                scale=ln_all[:, g, 0, k:k + 1],
                                                bias=ln_all[:, g, 1, k:k + 1])
                last.then_inc(h_done, 1)

            def split_h(g):
                act.wait_ge(h_transposed, g + 1)
                for c in range(DC):
                    nc.scalar.copy(hT_hi[:, c, g * CH:(g + 1) * CH], hT_ps[c][:]
                                   ).then_inc(hT_hi_done, 1)

            def split_g(g):
                for c in range(DC):
                    act.wait_ge(g_projected, DC * g + c + 1)
                    nc.scalar.activation(
                        gT[:, g * KT:(g + 1) * KT, 0, c, :],
                        gT_ps[c][:].rearrange("p (t q) -> p t q", t=KT), ACT.Identity,
                        bias=g_bias[:, c:c + 1]).then_inc(g_hi_done, 1)

            def split_v(g):
                for u in range(2):
                    act.wait_ge(v_projected, 2 * g + u + 1)
                    nc.scalar.copy(v_sb[:, g * KT + 2 * u:g * KT + 2 * u + 2, 0, :],
                                   v_ps[u][:].rearrange("p (t d) -> p t d", t=2)
                                   ).then_inc(v_hi_done, 1)

            normalise(0)
            normalise(1)
            split_h(0)
            normalise(2)
            act.wait_ge(scales_done, 1)
            nc.scalar.activation(m_hi[:], m_ps, ACT.Copy, scale=m_scale[:]).then_inc(weights_hi, 1)
            nc.scalar.activation(wvT_hi[:], wvT_ps, ACT.Copy, scale=wv_scale[:]
                                 ).then_inc(weights_hi, 1)
            for g in range(GROUPS):
                if g + 1 < GROUPS:
                    split_h(g + 1)
                split_g(g)
                split_v(g)
                if g + 3 < GROUPS:
                    normalise(g + 3)

            def scaled_ahead(pair, j):
                return not isinstance(pair, int) or chunk_no(pair, j) + SCALE_LEAD < SLOTS

            def scale_adj(pair, m):
                q, b = m % CHUNKS // 2, m // CHUNKS % 2
                act.wait_ge(adj_loaded[q], 16 * (tile_no(pair, m) + 1))
                piece = rows[b][:, q * PIECE:(q + 1) * PIECE]
                nc.scalar.activation(piece, piece, ACT.Copy, scale=adj_scale[:]
                                     ).then_inc(adj_scaled, 1)

            for m in range(0, SCALE_LEAD, 2):
                scale_adj(0, m)

            def slot(pair, j, runs):
                c = j % CHUNKS
                tile = tile_no(pair, j)
                b = j // CHUNKS % 2
                if runs(EXP_LAG):
                    if c == 0:
                        act.wait_ge(bias_done, tile)
                    w = rows[1 - b][:, c * CH:(c + 1) * CH]
                    nc.scalar.activation(w, w, ACT.Exp, scale=exp_scale[:], bias=exp_bias[1 - b][:],
                                         accum_out=chunk_sum[1 - b][:, c:c + 1]
                                         ).then_inc(exped, 1)
                if runs(HI_LAG):
                    at = j - HI_LAG
                    cols = slice(at % CHUNKS * CH, (at % CHUNKS + 1) * CH)
                    act.wait_ge(exped, chunk_no(pair, at) + 1)
                    wait(act, transposed[at % 2],
                         pair * (16 * UNROLL // 2) + 16 * ((at - SPLIT_RING) // 2 + 1))
                    nc.scalar.copy(w_split[:, at % SPLIT_RING, 0, :],
                                   rows[at // CHUNKS % 2][:, cols]).then_inc(split_hi, 1)
                if runs(TR_LAG):
                    at = j - TR_LAG
                    m = chunk_no(pair, at)
                    act.wait_ge(split_lo, m + 1)
                    wait(act, weighed, m - W_RING + 1)
                    wait(act, transposed[at % 2], pair * (16 * UNROLL // 2) + 16 * (at // 2))
                    act.sem_inc(transpose_released, 1)
                    act.dma_start_transpose(
                        wT[:, at % W_RING],
                        w_split[:, at % SPLIT_RING].rearrange("p s k -> p (s k)")
                        ).then_inc(transposed[at % 2], 16)
                if j % 2 == 0 and scaled_ahead(pair, j):
                    scale_adj(pair, j + SCALE_LEAD)
                if c == 2 and runs(0):
                    act.wait_ge(g_staged, tile + 1)
                    wait(act, r_done, tile)
                    nc.scalar.activation(h_tile[:],
                                         x_sb[:, bass.ds(tile, 1)].rearrange("p t d -> p (t d)"),
                                         ACT.Relu, scale=ln_tile[b][:, 0:1],
                                         bias=ln_tile[b][:, 1:2]).then_inc(h_again, 1)

            slots(act, slot, peel_last=True)

        @block.vector
        def _(dve):
            steps = [0]

            def link(ins):
                steps[0] += 1
                ins.then_inc(dve_step, 1)
                dve.wait_ge(dve_step, steps[0])

            def statistics(g):
                dve.wait_ge(x_loaded[g % 2], 16 * (g // 2 + 1))
                wait(dve, stats_done, g)
                for k in range(KT):
                    last = nc.vector.bn_stats(stats6[:, k, :], x_sb[:, g * KT + k, :])
                link(last)
                for k in range(KT):
                    last = nc.vector.bn_aggr(mean_var[:, k, :], stats6[:, k, :])
                link(last)
                wait(dve, ln_done, g - 1)
                nc.vector.tensor_scalar(neg_mean[:, g % 2], mean_var[:, :, 0], -1.0, None,
                                        ALU.mult)
                nc.vector.tensor_scalar(var_eps[:, g % 2], mean_var[:, :, 1], H_SCALE ** -2,
                                        EPS * H_SCALE ** -2, ALU.mult, ALU.add
                                        ).then_inc(stats_done, 1)

            def split_h(g):
                for c in range(DC):
                    dve.wait_ge(hT_hi_done, DC * g + c + 1)
                    nc.vector.tensor_tensor(hT_lo[:, c, g * CH:(g + 1) * CH], hT_ps[c][:],
                                            hT_hi[:, c, g * CH:(g + 1) * CH], ALU.subtract
                                            ).then_inc(hT_lo_done, 1)

            def split_g(g):
                for c in range(DC):
                    dve.wait_ge(g_hi_done, DC * g + c + 1)
                    nc.vector.scalar_tensor_tensor(
                        gT[:, g * KT:(g + 1) * KT, 1, c, :],
                        gT_ps[c][:].rearrange("p (t q) -> p t q", t=KT), g_bias[:, c:c + 1],
                        gT[:, g * KT:(g + 1) * KT, 0, c, :], ALU.add, ALU.subtract
                        ).then_inc(g_lo_done, 1)

            def split_v(g):
                for u in range(2):
                    dve.wait_ge(v_hi_done, 2 * g + u + 1)
                    pair = v_sb[:, g * KT + 2 * u:g * KT + 2 * u + 2]
                    nc.vector.tensor_tensor(pair[:, :, 1, :],
                                            v_ps[u][:].rearrange("p (t d) -> p t d", t=2),
                                            pair[:, :, 0, :], ALU.subtract).then_inc(v_lo_done, 1)

            dve.wait_ge(wqk_loaded, 64)
            dve.wait_ge(ones_set, 1)
            for c in range(DC):
                last = nc.vector.tensor_scalar(bk_wide[:, c, :], ones[:], bk_sb[:, c:c + 1], None,
                                               ALU.mult)
            last.then_inc(bk_widened, 1)
            statistics(0)
            statistics(1)
            statistics(2)

            dve.wait_ge(m_done, 1)
            nc.vector.tensor_reduce(tops[:, 0:1], bank[6][:], AX.X, ALU.max,
                                    apply_absolute_value=True)
            dve.wait_ge(small_done, 1)
            nc.vector.tensor_reduce(tops[:, 1:2], small_ps[:, D:D + DC], AX.X, ALU.max,
                                    apply_absolute_value=True)
            nc.vector.tensor_copy(wqbk_row[:], small_ps[:, 0:D])
            nc.vector.tensor_scalar(rbias0[:], small_ps[:, D + DC:D + DC + 1], SCORE_SCALE, None,
                                    ALU.mult)
            dve.wait_ge(wvT_done, 1)
            nc.vector.tensor_reduce(tops[:, 2:3], bank[0][:], AX.X, ALU.max,
                                    apply_absolute_value=True).then_inc(tops_done, 1)
            dve.wait_ge(tops_shared, 1)
            link(nc.vector.scalar_tensor_tensor(bound[:, 0:1], all_tops[:, 0:1], H_L1,
                                                all_tops[:, 1:2], ALU.mult, ALU.add))
            link(nc.vector.tensor_scalar(bound[:, 1:2], all_tops[:, 2:3], H_L1, None, ALU.mult))
            link(nc.vector.tensor_scalar(bound[:], bound[:], LEAST_BOUND, None, ALU.max))
            link(nc.vector.tensor_scalar(power[:].bitcast(U32), bound[:].bitcast(U32), 0x7F800000,
                                         None, ALU.bitwise_and))
            link(nc.vector.reciprocal(inv_power[:], power[:]))
            nc.vector.tensor_scalar(kappa[:], inv_power[:, 0:1], G_TOP, None, ALU.mult)
            nc.vector.tensor_scalar(m_scale[:], inv_power[:, 0:1], G_TOP / H_SCALE, None, ALU.mult)
            nc.vector.tensor_scalar(wv_scale[:], inv_power[:, 1:2], V_TOP / H_SCALE, None, ALU.mult)
            nc.vector.tensor_scalar(adj_scale[:], inv_power[:, 0:1],
                                    2 * G_TOP * H_SCALE / SCORE_SCALE, None, ALU.mult)
            nc.vector.tensor_scalar(exp_scale[:], power[:, 0:1], SCORE_SCALE / (G_TOP * H_SCALE),
                                    None, ALU.mult)
            link(nc.vector.tensor_scalar(inv_omega[:], power[:, 1:2], 1.0 / V_TOP, None, ALU.mult))
            nc.vector.tensor_scalar(g_bias[:], small_ps[:, D:D + DC], kappa[:], None, ALU.mult
                                    ).then_inc(scales_done, 1)
            dve.wait_ge(weights_hi, 2)
            nc.vector.scalar_tensor_tensor(m_lo[:].rearrange("p c d -> p (c d)"), bank[6][:],
                                           m_scale[:], m_hi[:].rearrange("p c d -> p (c d)"),
                                           ALU.mult, ALU.subtract)
            nc.vector.scalar_tensor_tensor(wvT_lo[:].rearrange("p c d -> p (c d)"), bank[0][:],
                                           wv_scale[:], wvT_hi[:].rearrange("p c d -> p (c d)"),
                                           ALU.mult, ALU.subtract).then_inc(weights_lo, 1)
            split_h(0)
            statistics(3)
            for g in range(GROUPS):
                if g + 1 < GROUPS:
                    split_h(g + 1)
                split_g(g)
                split_v(g)
                if g + 4 < GROUPS:
                    statistics(g + 4)

            def slot(pair, j, runs):
                c = j % CHUNKS
                tile = tile_no(pair, j)
                b = j // CHUNKS % 2
                if runs(0):
                    dve.wait_ge(adj_scaled, pair * (UNROLL // 2) + j // 2 + 1)
                    dve.wait_ge(scored, chunk_no(pair, j) + 1)
                if runs(LO_LAG):
                    at = j - LO_LAG
                    cols = slice(at % CHUNKS * CH, (at % CHUNKS + 1) * CH)
                    w = w_split[:, at % SPLIT_RING]
                    dve.wait_ge(split_hi, chunk_no(pair, at) + 1)
                    nc.vector.tensor_tensor(w[:, 1, :], rows[at // CHUNKS % 2][:, cols],
                                            w[:, 0, :], ALU.subtract
                                            ).then_inc(split_lo, 1)
                if runs(0):
                    a = rows[b][:, c * CH:(c + 1) * CH]
                    nc.vector.tensor_tensor_reduce(
                        out=a, in0=score_ps[j % SCORE_BANKS][:], in1=a, scale=1.0,
                        scalar=-3.0e38, op0=ALU.add, op1=ALU.max,
                        accum_out=chunk_max[b][:, c:c + 1]).then_inc(summed, 1)
                    if c == 4:
                        dve.wait_ge(h_again, tile + 1)
                        nc.vector.tensor_tensor_reduce(
                            out=h_tile[:], in0=h_tile[:], in1=wqbk_row[:],
                            scale=SCORE_SCALE / H_SCALE, scalar=rbias0[:], op0=ALU.mult,
                            op1=ALU.add, accum_out=r_row[:]).then_inc(r_done, 1)
                    if c == CHUNKS - 1:
                        dve.wait_ge(summed, chunk_no(pair, j) + 1)
                        nc.vector.reduce_max(tile_max[:], chunk_max[b][:], AX.X
                                             ).then_inc(max_step, 1)
                        dve.wait_ge(max_step, tile * 2 + 1)
                        dve.wait_ge(r_done, tile + 1)
                        nc.vector.scalar_tensor_tensor(row_max[:], tile_max[:], exp_scale[:],
                                                       r_row[:], ALU.mult, ALU.add
                                                       ).then_inc(max_step, 1)
                        dve.wait_ge(max_step, tile * 2 + 2)
                        wait(dve, exped, CHUNKS * (tile - 1))
                        nc.vector.scalar_tensor_tensor(exp_bias[b][:], r_row[:], LN_P_SCALE,
                                                       row_max[:], ALU.add, ALU.subtract
                                                       ).then_inc(bias_done, 1)
                        dve.wait_ge(bias_done, tile + 1)
                if c == FINISH_AT and runs(2 * CHUNKS + FINISH_AT):
                    finish(tile - 2, b)

            def finish(t, parity):
                dve.wait_ge(exped, CHUNKS * (t + 1))
                nc.vector.reduce_sum(row_sum[:], chunk_sum[parity][:], AX.X).then_inc(fin_step, 1)
                dve.wait_ge(fin_step, t * 4 + 1)
                nc.vector.reciprocal(inv_sum[:], row_sum[:]).then_inc(fin_step, 1)
                dve.wait_ge(fin_step, 4 * t + 2)
                nc.vector.tensor_tensor(out_scale[:], inv_sum[:], inv_omega[:], ALU.mult
                                        ).then_inc(fin_step, 1)
                dve.wait_ge(fin_step, 4 * t + 3)
                dve.wait_ge(weighed, CHUNKS * (t + 1))
                dve.wait_ge(xb_done, t + 1)
                nc.vector.scalar_tensor_tensor(half_out[:], o_ps[parity][:, D:2 * D], out_scale[:],
                                               x_bias[parity][:], ALU.mult, ALU.add
                                               ).then_inc(fin_step, 1)
                dve.wait_ge(fin_step, 4 * t + 4)
                nc.vector.scalar_tensor_tensor(y[parity][:], o_ps[parity][:, 0:D], out_scale[:],
                                               half_out[:], ALU.mult, ALU.add
                                               ).then_inc(y_done, 1)
                dve.wait_ge(y_done, t + 1)

            slots(dve, slot)
            finish(TILES - 1, (TILES - 1) % 2)

        @block.tensor
        def _(pe):
            def matmul(out_ap, stationary, moving, first, last):
                return nc.tensor.matmul(out_ap, stationary, moving, start=first, stop=last)

            pe.wait_ge(wqk_loaded, 64)
            for c in range(DC):
                for e in range(DC):
                    last = matmul(m_ps[:, c, :], wq_sb[:, e, c * P:(c + 1) * P], wk_sb[:, e, :],
                                  e == 0, e == DC - 1)
            last.then_inc(m_done, 1)
            for c in range(DC):
                for e in range(DC):
                    matmul(small_ps[:, D + c:D + c + 1], wk_sb[:, e, c * P:(c + 1) * P],
                           bq_sb[:, e:e + 1], e == 0, e == DC - 1)
            pe.wait_ge(bk_widened, 1)
            for e in range(DC):
                matmul(small_ps[:, 0:D], bk_wide[:, e, :], wq_sb[:, e, :], e == 0, e == DC - 1)
            for e in range(DC):
                last = matmul(small_ps[:, D + DC:D + DC + 1], bk_wide[:, e, :], bq_sb[:, e:e + 1],
                              e == 0, e == DC - 1)
            last.then_inc(small_done, 1)
            pe.wait_ge(wv_loaded, 16)
            pe.wait_ge(ident_set, 1)
            for c in range(DC):
                for e in range(DC):
                    last = nc.tensor.transpose(wvT_ps[:, c, e * P:(e + 1) * P],
                                               wv_sb[:, e, c * P:(c + 1) * P], ident[:])
            last.then_inc(wvT_done, 1)

            def transpose_h(g):
                pe.wait_ge(h_done, g + 1)
                if g >= 1:
                    pe.wait_ge(hT_lo_done, DC * g)
                for c in range(DC):
                    for k in range(KT):
                        last = nc.tensor.transpose(hT_ps[c][:, k * P:(k + 1) * P],
                                                   h_grp[:, g % 2, k, c * P:(c + 1) * P], ident[:])
                last.then_inc(h_transposed, 1)

            def three_products(out_ap, parts):
                for i, (a_hi, a_lo, b_hi, b_lo) in enumerate(parts):
                    matmul(out_ap, a_hi, b_hi, i == 0, False)
                    matmul(out_ap, a_hi, b_lo, False, False)
                    last = matmul(out_ap, a_lo, b_hi, False, i == len(parts) - 1)
                return last

            def project(g):
                pe.wait_ge(hT_lo_done, DC * (g + 1))
                keys = slice(g * CH, (g + 1) * CH)
                for c in range(DC):
                    cols = slice(c * P, (c + 1) * P)
                    wait(pe, g_lo_done, DC * (g - 1) + c + 1)
                    three_products(gT_ps[c][:],
                                   [(m_hi[:, k, cols], m_lo[:, k, cols],
                                     hT_hi[:, k, keys], hT_lo[:, k, keys]) for k in range(DC)]
                                   ).then_inc(g_projected, 1)
                for u in range(2):
                    wait(pe, v_lo_done, 2 * (g - 1) + u + 1)
                    for w in range(2):
                        k0 = g * CH + (2 * u + w) * P
                        last = three_products(
                            v_ps[u][:, w * D:(w + 1) * D],
                            [(hT_hi[:, k, k0:k0 + P], hT_lo[:, k, k0:k0 + P],
                              wvT_hi[:, k, :], wvT_lo[:, k, :]) for k in range(DC)])
                    last.then_inc(v_projected, 1)

            transpose_h(0)
            pe.wait_ge(weights_lo, 1)
            for g in range(GROUPS):
                if g + 1 < GROUPS:
                    transpose_h(g + 1)
                project(g)
            pe.wait_ge(g_lo_done, DC * GROUPS)
            pe.wait_ge(v_lo_done, 2 * GROUPS)

            def score(pair, j):
                c = j % CHUNKS
                b = j // CHUNKS % 2
                tile = tile_no(pair, j)
                if c == 0:
                    pe.wait_ge(g_staged, tile + 1)
                wait(pe, summed, chunk_no(pair, j) - SCORE_BANKS + 1)
                keys = slice(c * CH, (c + 1) * CH)
                g = g_tile[b]
                three_products(score_ps[j % SCORE_BANKS][:],
                               [(g[:, 0, k, :], g[:, 1, k, :], hT_hi[:, k, keys],
                                 hT_lo[:, k, keys]) for k in range(DC)]).then_inc(scored, 1)

            def weigh(pair, j):
                c, b, at = j % CHUNKS, j // CHUNKS % 2, j % W_RING
                pe.wait_ge(transposed[j % 2], pair * (16 * UNROLL // 2) + 16 * (j // 2 + 1))
                for k in range(KT):
                    kt = c * KT + k
                    matmul(o_ps[b][:], wT[:, at, k, :],
                           v_sb[:, kt].rearrange("p s d -> p (s d)"), kt == 0, False)
                    last = matmul(o_ps[b][:, 0:D], wT[:, at, KT + k, :],
                                  v_sb[:, kt, 0, :], False, kt == CHUNKS * KT - 1)
                last.then_inc(weighed, 1)

            def slot(pair, j, runs):
                if runs(0):
                    score(pair, j)
                if runs(V_LAG):
                    weigh(pair, j - V_LAG)

            slots(pe, slot)


_INS = ['x', 'adj', 'L0_gnn_Wq', 'L0_gnn_bq', 'L0_gnn_Wk', 'L0_gnn_bk', 'L0_gnn_Wv', 'L0_gnn_bv']


def kernel(**inputs):
    import numpy as _np
    import concourse.bacc as _bacc
    from concourse.bass_utils import run_bass_kernel_spmd as _run

    nc = _bacc.Bacc("TRN2", target_bir_lowering=False, num_devices=1)
    arrays, args = {}, []
    for name in _INS:
        a = _np.ascontiguousarray(inputs[name])
        arrays[f"in_{name}"] = a
        args.append(nc.dram_tensor(f"in_{name}", a.shape, mybir.dt.from_np(a.dtype),
                                   kind="ExternalInput").ap())
    result = nc.dram_tensor("out_y", (N, D), FP32, kind="ExternalOutput").ap()
    attention_kernel(nc, *args, result)
    r = _run(nc, [arrays], core_ids=[0])
    return r.results[0]["out_y"]
```
